# Optimizing a Trainium2 kernel written in Bass

```python
import numpy as np
import jax
import jax.numpy as jnp

def _softmax(x, axis=-1):
    return jax.nn.softmax(x, axis=axis)

def _gelu(x):
    return jax.nn.gelu(x, approximate=True)

def _silu(x):
    return jax.nn.silu(x)

def _sigmoid(x):
    return jax.nn.sigmoid(x)

def _layernorm(x, axis=-1, eps=1e-05):
    m = jnp.mean(x, axis=axis, keepdims=True)
    v = jnp.var(x, axis=axis, keepdims=True)
    return (x - m) / jnp.sqrt(v + eps)

def _scatter_add(tgt, idx, src, axis=0):
    return tgt.at[idx].add(src)

def _segment_sum(src, seg, n):
    return jax.ops.segment_sum(src, seg, n)
kernel_name = 'mk_cond_seq_d1_seqx_r4_61c717'

def setup_inputs(seed: int=0):
    np.random.seed(seed)
    _w = jnp.asarray

    def _rec_inputs():
        import jax
        import jax.numpy as jnp
        _rk = jax.random.key(seed)
        x = 7.22e-05 + 1 * jax.random.normal(jax.random.fold_in(_rk, 1), (128, 64, 256), jnp.float32)
        _lenS = 64 - jax.random.randint(jax.random.fold_in(_rk, 7), (128,), 0, max(1, 64 // 4) + 1, jnp.int32)
        _lenS2 = 64 - jax.random.randint(jax.random.fold_in(_rk, 8), (128,), 0, max(1, 64 // 4) + 1, jnp.int32)
        cond_2048 = 0.00782532 + 1.00527 * jax.random.normal(jax.random.fold_in(_rk, 11), (128, 512), jnp.float32)
        _validS = jnp.arange(64)[None, :] < _lenS[:, None]
        _validS2 = jnp.arange(64)[None, :] < _lenS2[:, None]
        _causal = jnp.tril(jnp.ones((64, 64), dtype=bool))
        mask_BxSx1_fk1 = jnp.where(jnp.ones((128, 64, 1), dtype=bool), 1.0, 0.0).astype(jnp.float32)
        return (x, cond_2048, mask_BxSx1_fk1)
    x, cond_2048, mask_BxSx1_fk1 = _rec_inputs()

    def _L0_cond_setup():
        import jax, jax.numpy as jnp
        import numpy as np
        B, T, D, H, TE = (4, 512, 256, 8, 512)
        EPS = 1e-05

        def _ln(x, w, b):
            m = jnp.mean(x, axis=-1, keepdims=True)
            v = jnp.mean((x - m) ** 2, axis=-1, keepdims=True)
            return (x - m) * jax.lax.rsqrt(v + EPS) * w + b
        key = jax.random.key(seed)
        ks = jax.random.split(key, 16)
        s = 0.02
        inp = {'x': jax.random.normal(ks[0], (B, T, D), jnp.float32), 'emb': jax.random.normal(ks[1], (B, TE), jnp.float32), 'src_mask': (jax.random.uniform(ks[2], (B, T, 1)) > 0.2).astype(jnp.float32), 'num_head': H, 'ln_w': jnp.ones((D,), jnp.float32), 'ln_b': jnp.zeros((D,), jnp.float32), 'Wq': jax.random.normal(ks[3], (D, D), jnp.float32) * s, 'bq': jnp.zeros((D,), jnp.float32), 'Wk': jax.random.normal(ks[4], (D, D), jnp.float32) * s, 'bk': jnp.zeros((D,), jnp.float32), 'Wv': jax.random.normal(ks[5], (D, D), jnp.float32) * s, 'bv': jnp.zeros((D,), jnp.float32), 'W_emb': jax.random.normal(ks[6], (TE, 2 * D), jnp.float32) * s, 'b_emb': jnp.zeros((2 * D,), jnp.float32), 'ln2_w': jnp.ones((D,), jnp.float32), 'ln2_b': jnp.zeros((D,), jnp.float32), 'W_out': jax.random.normal(ks[7], (D, D), jnp.float32) * s, 'b_out': jnp.zeros((D,), jnp.float32)}
        return inp
    _L0_cond_all = _L0_cond_setup()
    _L0_cond_in = {k: v for k, v in _L0_cond_all.items() if k in ('ln_w', 'ln_b', 'Wq', 'bq', 'Wk', 'bk', 'Wv', 'bv', 'W_emb', 'b_emb', 'ln2_w', 'ln2_b', 'W_out', 'b_out')}
    del _L0_cond_all
    return {'x': x, 'cond_2048': cond_2048, 'mask_BxSx1_fk1': mask_BxSx1_fk1, 'L0_cond_ln_w': _L0_cond_in['ln_w'], 'L0_cond_ln_b': _L0_cond_in['ln_b'], 'L0_cond_Wq': _L0_cond_in['Wq'], 'L0_cond_bq': _L0_cond_in['bq'], 'L0_cond_Wk': _L0_cond_in['Wk'], 'L0_cond_bk': _L0_cond_in['bk'], 'L0_cond_Wv': _L0_cond_in['Wv'], 'L0_cond_bv': _L0_cond_in['bv'], 'L0_cond_W_emb': _L0_cond_in['W_emb'], 'L0_cond_b_emb': _L0_cond_in['b_emb'], 'L0_cond_ln2_w': _L0_cond_in['ln2_w'], 'L0_cond_ln2_b': _L0_cond_in['ln2_b'], 'L0_cond_W_out': _L0_cond_in['W_out'], 'L0_cond_b_out': _L0_cond_in['b_out']}

def reference(x, cond_2048, mask_BxSx1_fk1, L0_cond_ln_w, L0_cond_ln_b, L0_cond_Wq, L0_cond_bq, L0_cond_Wk, L0_cond_bk, L0_cond_Wv, L0_cond_bv, L0_cond_W_emb, L0_cond_b_emb, L0_cond_ln2_w, L0_cond_ln2_b, L0_cond_W_out, L0_cond_b_out):
    import jax
    import jax.numpy as jnp

    def _L0_cond_ref(x, emb, src_mask, num_head, ln_w, ln_b, Wq, bq, Wk, bk, Wv, bv, W_emb, b_emb, ln2_w, ln2_b, W_out, b_out):
        import jax, jax.numpy as jnp
        import numpy as np
        B, T, D, H, TE = (4, 512, 256, 8, 512)
        EPS = 1e-05

        def _ln(x, w, b):
            m = jnp.mean(x, axis=-1, keepdims=True)
            v = jnp.mean((x - m) ** 2, axis=-1, keepdims=True)
            return (x - m) * jax.lax.rsqrt(v + EPS) * w + b
        b, t, d = x.shape
        h = num_head
        dh = d // h
        xn = _ln(x, ln_w, ln_b)
        q = xn @ Wq + bq
        k = xn @ Wk + bk + (1.0 - src_mask) * -1000000.0
        q = jax.nn.softmax(q.reshape(b, t, h, dh), axis=-1)
        k = jax.nn.softmax(k.reshape(b, t, h, dh), axis=1)
        v = ((xn @ Wv + bv) * src_mask).reshape(b, t, h, dh)
        att = jnp.einsum('bnhd,bnhl->bhdl', k, v)
        y = jnp.einsum('bnhd,bhdl->bnhl', q, att).reshape(b, t, d)
        emb_out = (jax.nn.silu(emb) @ W_emb + b_emb)[:, None, :]
        scale, shift = jnp.split(emb_out, 2, axis=2)
        hh = _ln(y, ln2_w, ln2_b) * (1.0 + scale) + shift
        hh = jax.nn.silu(hh) @ W_out + b_out
        return x + hh
    x = _L0_cond_ref(x, cond_2048, mask_BxSx1_fk1, 8, L0_cond_ln_w, L0_cond_ln_b, L0_cond_Wq, L0_cond_bq, L0_cond_Wk, L0_cond_bk, L0_cond_Wv, L0_cond_bv, L0_cond_W_emb, L0_cond_b_emb, L0_cond_ln2_w, L0_cond_ln2_b, L0_cond_W_out, L0_cond_b_out)
    return x

_drawn_inputs = setup_inputs


def setup_inputs(seed=0):
    import zlib

    import numpy as np

    out = dict(_drawn_inputs(seed))
    spreads = {'L0_cond_ln_w': (1.0, 0.6),
     'L0_cond_ln_b': (0.0, 0.1),
     'L0_cond_bq': (0.0, 0.8),
     'L0_cond_bk': (0.0, 0.8),
     'L0_cond_bv': (0.0, 0.1),
     'L0_cond_b_emb': (0.0, 0.1),
     'L0_cond_ln2_w': (1.0, 0.2),
     'L0_cond_ln2_b': (0.0, 0.464),
     'L0_cond_b_out': (0.0, 0.1)}
    factors = {'L0_cond_Wq': 8.0, 'L0_cond_Wk': 8.0}
    for name, (base, spread) in spreads.items():
        noise = np.random.default_rng([zlib.crc32(name.encode()), seed]).standard_normal(out[name].shape)
        drawn = base * np.exp(spread * noise) if base else spread * noise
        out[name] = jnp.asarray(drawn.astype(out[name].dtype))
    for name, factor in factors.items():
        out[name] = (out[name] * factor).astype(out[name].dtype)
    return out
```

```python
import numpy as np
import concourse.bass as bass
from concourse import mybir
from contextlib import ExitStack


def build_layer(nc, x, cond_t, mask_cols, mask_rows, ln_w, ln_b, wq, bq, wk, bk, wv, bv, w_emb, b_emb,
                ln2_w, ln2_b, w_out, b_out, out):
    fp32 = mybir.dt.float32
    f32r = mybir.dt.float32r
    ALU = mybir.AluOpType
    ACT = mybir.ActivationFunctionType
    AX = mybir.AxisListType

    P = 128
    ROWS, D = x.shape
    BATCH, SEQ = mask_rows.shape
    HEADS = 8
    DH = D // HEADS
    C = D // P
    HC = HEADS // C
    GT = 512
    G = ROWS // GT
    T = GT // P
    GB = GT // SEQ
    E = cond_t.shape[0]
    EC = E // P
    AW = DH + 1
    EPS = 1e-5

    ctx = ExitStack()
    with ctx:
        def sb(name, shape, dt=fp32):
            return ctx.enter_context(nc.sbuf_tensor(name, shape, dt))

        def sem(name):
            return ctx.enter_context(nc.semaphore(name))

        x_all = sb("x_all", [P, G, T * D])
        w_qv_hi = sb("w_qv_hi", [P, C, 2 * D], f32r)
        w_qv_lo = sb("w_qv_lo", [P, C, 2 * D], f32r)
        w_k_hi = sb("w_k_hi", [P, C, D], f32r)
        w_k_lo = sb("w_k_lo", [P, C, D], f32r)
        w_o_hi = sb("w_o_hi", [P, C, D], f32r)
        w_o_lo = sb("w_o_lo", [P, C, D], f32r)
        bo_all = sb("bo_all", [P, D])
        ident = sb("ident", [P, P])
        mod_scale = sb("mod_scale", [P, C, BATCH])
        mod_shift = sb("mod_shift", [P, C, BATCH])
        mask_c = sb("mask_c", [P, ROWS // P])
        n_row = sb("n_row", [2, ROWS], f32r)
        ones2 = sb("ones2", [2, P], f32r)
        neg_half = sb("neg_half", [P, T])

        emb = sb("emb", [P, 2 * C, BATCH])
        lnw = sb("lnw", [P, C])
        lnb = sb("lnb", [P, C])
        ln2w = sb("ln2w", [P, C])
        ln2b = sb("ln2b", [P, C])
        b_e = sb("b_e", [P, 2 * C])
        brow = sb("brow", [1, 3 * D])
        fold = sb("fold", [P, C, P])
        inv_row = sb("inv_row", [1, P])
        mask_r = sb("mask_r", [P, SEQ])
        n_hi = sb("n_hi", [P, SEQ], f32r)
        n_lo = sb("n_lo", [P, SEQ], f32r)

        xstat = sb("xstat", [P, T, 6])
        xmv = sb("xmv", [P, T, 2])
        xr = sb("xr", [P, 4, T])
        xhat = sb("xhat", [P, 2, T, D])
        xt_hi = sb("xt_hi", [P, C, GT], f32r)
        xt_lo = sb("xt_lo", [P, C, GT], f32r)
        kmax = sb("kmax", [P, C, GB])
        k_t = sb("k_t", [P, 2, C, GT])
        qmax = sb("qmax", [P, T, HEADS])
        q_s = sb("q_s", [P, 2, T, D])
        v_s = sb("v_s", [P, 2, T, HEADS, AW])
        e_k = sb("e_k", [P, T, D])
        kv = sb("kv", [P, GB, C, HC * AW])
        rk = sb("rk", [P, 2, GB // 2, C])
        q_t = sb("q_t", [P, C, GT])
        rq = sb("rq", [P, T, HEADS])
        y_s = sb("y_s", [P, T, D])
        ystat = sb("ystat", [P, T, 6])
        ymv = sb("ymv", [P, T, 2])
        yr = sb("yr", [P, 4, T])
        z_s = sb("z_s", [P, C, GT])
        th = sb("th", [P, C, GT])
        h_s = sb("h_s", [P, C, GT])
        h_hi = sb("h_hi", [P, C, GT], f32r)
        h_lo = sb("h_lo", [P, C, GT], f32r)

        w_qv = q_t
        w_o = y_s[:, 0:C, :]
        w_k = y_s[:, C:2 * C, :]
        w_e = k_t[:, :, :, :].rearrange("p a c n -> p (a c) n")
        cond = th[:, 0, :].rearrange("p (c b) -> p c b", c=EC)
        tanh_c = th[:, 1, :].rearrange("p (c b) -> p c b", c=EC)

        def bank(name):
            return ctx.enter_context(nc.psum_tensor(name, [P, 512], fp32))
        bt = [bank("bt0"), bank("bt1")]
        be = [bank("be0"), bank("be1")]
        bk_ = [bank("bk0"), bank("bk1")]
        bv_ = [bank("bv0"), bank("bv1")]
        bqv = bv_ + bk_

        w_in = sem("w_in")
        m_in = sem("m_in")
        c_in = sem("c_in")
        n_rows_in = sem("n_rows_in")
        x_in = [sem("x_in0"), sem("x_in1")]
        stored = sem("stored")
        pool_init = sem("pool_init")
        id_zero = sem("id_zero")
        fold_ready = sem("fold_ready")
        beta_done = sem("beta_done")
        tanh_c_ready = sem("tanh_c_ready")
        silu_c_ready = sem("silu_c_ready")
        emb_done = sem("emb_done")
        n_ready = sem("n_ready")
        setup_v = sem("setup_v")
        weights_ready = sem("weights_ready")
        mod_ready = sem("mod_ready")
        xstat_d = sem("xstat_d")
        xmv_d = sem("xmv_d")
        xr_d = sem("xr_d")
        xhat_d = sem("xhat_d")
        xt_d = sem("xt_d")
        hi_d = sem("hi_d")
        lo_d = sem("lo_d")
        k_d = sem("k_d")
        kmax_d = sem("kmax_d")
        ksub_d = sem("ksub_d")
        kexp_d = sem("kexp_d")
        qv_d = sem("qv_d")
        v_d = sem("v_d")
        qmax_d = sem("qmax_d")
        qsub_d = sem("qsub_d")
        qexp_d = sem("qexp_d")
        ekt_d = sem("ekt_d")
        ek_d = sem("ek_d")
        att_d = sem("att_d")
        rk_d = sem("rk_d")
        kv_d = sem("kv_d")
        eqt_d = sem("eqt_d")
        qt_d = sem("qt_d")
        y_d = sem("y_d")
        rq_d = sem("rq_d")
        ys_d = sem("ys_d")
        ystat_d = sem("ystat_d")
        ymv_d = sem("ymv_d")
        yr_d = sem("yr_d")
        yhat_d = sem("yhat_d")
        yhat_a_d = sem("yhat_a_d")
        yt_d = sem("yt_d")
        zs_d = sem("zs_d")
        z_d = sem("z_d")
        th_d = sem("th_d")
        h_d = sem("h_d")
        hhi_d = sem("hhi_d")
        hlo_d = sem("hlo_d")
        xb_d = sem("xb_d")
        o_d = sem("o_d")
        res_d = sem("res_d")

        block = ctx.enter_context(nc.Block())

        def wait(eng, s, n):
            if isinstance(n, int) and n <= 0:
                return
            eng.wait_ge(s, n)

        def wait_apart(eng, s, n):
            wait(eng, s, n)
            if not isinstance(n, int):
                eng.nop(nofuse=True)

        def steps(eng, body):
            def at(i):
                body(i, i % 2, i + 1 < G, 0 <= i < G, 0 <= i - 1 < G, 0 <= i - 2 < G)
            for i in (-1, 0, 1, 2):
                at(i)
            with eng.Fori(1, G // 2 - 1) as turn:
                body(2 * turn + 1, 1, True, True, True, True)
                body(2 * turn + 2, 0, True, True, True, True)
            for i in range(G - 1, G + 2):
                at(i)

        x_h = x.rearrange("(g t p) d -> g p t d", t=T, p=P)
        o_h = out.rearrange("(g t p) d -> g p t d", t=T, p=P)

        def group_of(tensor, g):
            return tensor[:, g:g + 1, :] if isinstance(g, int) else tensor[:, bass.ds(g, 1), :]

        def span(g, n):
            return slice(g * n, g * n + n) if isinstance(g, int) else bass.ds(g * n, n)

        @block.sync
        def _(sp):
            def load_x(g, parity):
                sp.dma_start(group_of(x_all, g).rearrange("p g (t d) -> p (g t) d", t=T),
                             x_h[span(g, 1)].rearrange("g p t d -> p (g t) d")).then_inc(x_in[parity], 16)

            load_x(0, 0)
            sp.dma_start(w_qv[:, :, 0:D], wq.rearrange("(c p) n -> p c n", p=P)).then_inc(w_in, 16)
            sp.dma_start(w_qv[:, :, D:2 * D], wv.rearrange("(c p) n -> p c n", p=P)).then_inc(w_in, 16)
            sp.dma_start(w_k, wk.rearrange("(c p) n -> p c n", p=P)).then_inc(w_in, 16)
            load_x(1, 1)
            sp.dma_start(w_o, w_out.rearrange("(c p) n -> p c n", p=P)).then_inc(w_in, 16)
            sp.dma_start(bo_all[:, :], b_out[None, :].broadcast_to([P, D])).then_inc(w_in, 16)

            def store(g):
                wait(sp, res_d, 2 * g + 2)
                sp.dma_start(o_h[span(g, 1)].rearrange("g p t d -> p (g t) d"),
                             group_of(x_all, g).rearrange("p g (t d) -> p (g t) d", t=T)).then_inc(stored, 16)

            def body(i, par, N, F, B, O):
                if N and not (isinstance(i, int) and i < 1):
                    wait(sp, xstat_d, 4 * i)
                    load_x(i + 1, 1 - par)
                if O and not (isinstance(i, int) and i < 3):
                    store(i - 3)

            steps(sp, body)
            store(G - 1)
            sp.wait_ge(stored, 16 * G)

        @block.gpsimd
        def _(pool):
            for dst, src in ((lnw, ln_w), (lnb, ln_b), (ln2w, ln2_w), (ln2b, ln2_b), (b_e, b_emb)):
                pool.dma_start(dst[:, :], src).then_inc(m_in, 16)
            pool.dma_start(brow[:, 0:D], bq[None, :]).then_inc(m_in, 16)
            pool.dma_start(brow[:, D:2 * D], bv[None, :]).then_inc(m_in, 16)
            pool.dma_start(brow[:, 2 * D:3 * D], bk[None, :]).then_inc(m_in, 16)
            pool.dma_start(mask_c[:, :], mask_cols).then_inc(m_in, 16)
            pool.dma_start(mask_r[:, :], mask_rows).then_inc(m_in, 16)
            pool.memset(ident[:, :], 0.0).then_inc(id_zero, 1)
            pool.memset(neg_half[:, :], -0.5).then_inc(pool_init, 1)
            pool.wait_ge(id_zero, 1)
            pool.affine_select(out=ident[:, :], in_=ident[:, :], compare_op=ALU.not_equal, fill=1.0, base=0,
                               pattern=[[-1, P]], channel_multiplier=1).then_inc(pool_init, 1)
            pool.memset(inv_row[:, :], 1.0 / D).then_inc(pool_init, 1)
            pool.memset(ones2[:, :].bitcast(fp32), 1.0).then_inc(pool_init, 1)
            pool.memset(v_s[:, :, :, :, DH:AW], 1.0).then_inc(pool_init, 1)
            pool.memset(kv[:, :, :, :], 0.0).then_inc(pool_init, 1)

            def body(i, par, N, F, B, O):
                if O:
                    g = i - 2
                    if isinstance(g, int) and g == 0:
                        pool.wait_ge(mod_ready, C)
                    for c in range(C):
                        wait(pool, zs_d, 2 * g + c + 1)
                        nc.gpsimd.tensor_tensor(
                            z_s[:, c, :].rearrange("p (b s) -> p b s", s=SEQ),
                            z_s[:, c, :].rearrange("p (b s) -> p b s", s=SEQ),
                            mod_shift[:, c, span(g, GB)].unsqueeze(2).broadcast_to([P, GB, SEQ]),
                            ALU.add).then_inc(z_d, 1)
                if N:
                    g = i + 1
                    if isinstance(g, int) and g == 0:
                        pool.wait_ge(pool_init, 1)
                    wait(pool, xhat_d, 4 * g)
                    wait_apart(pool, xmv_d, 4 * g + 4)
                    nc.gpsimd.tensor_scalar(xr[:, 0, :], xmv[:, :, 1], 1.0, EPS, ALU.mult, ALU.add).then_inc(xr_d, 1)
                    wait(pool, xr_d, 4 * g + 1)
                    nc.gpsimd.tensor_tensor(xr[:, 1, :], xr[:, 0, :], neg_half[:, :], ALU.pow).then_inc(xr_d, 1)
                    wait(pool, xr_d, 4 * g + 2)
                    nc.gpsimd.tensor_tensor(xr[:, 2, :], xmv[:, :, 0], xr[:, 1, :], ALU.mult).then_inc(xr_d, 1)
                    wait_apart(pool, xr_d, 4 * g + 3)
                    nc.gpsimd.tensor_scalar(xr[:, 3, :], xr[:, 2, :], -1.0, 1.0, ALU.mult, ALU.add).then_inc(xr_d, 1)
                if F:
                    g = i
                    if isinstance(g, int) and g == 0:
                        pool.wait_ge(w_in, 80)
                    wait(pool, xhat_d, 4 * g + 4)
                    xg = group_of(x_all, g).rearrange("p g (t d) -> p (g t) d", t=T)
                    nc.gpsimd.tensor_tensor(xg, xg, bo_all[:, :].unsqueeze(1).broadcast_to([P, T, D]),
                                            ALU.add).then_inc(xb_d, 1)
                if O:
                    g = i - 2
                    for c in range(C):
                        wait(pool, hhi_d, 2 * g + c + 1)
                        wait(pool, o_d, 2 * g)
                        nc.gpsimd.tensor_tensor(h_lo[:, c, :], h_s[:, c, :], h_hi[:, c, :].bitcast(fp32),
                                                ALU.subtract).then_inc(hlo_d, 1)
                if B:
                    g = i - 1
                    wait(pool, yhat_d, 2 * g)
                    wait(pool, yhat_a_d, 2 * g)
                    wait_apart(pool, ymv_d, 4 * g + 4)
                    nc.gpsimd.tensor_scalar(yr[:, 0, :], ymv[:, :, 1], 1.0, EPS, ALU.mult, ALU.add).then_inc(yr_d, 1)
                    wait(pool, yr_d, 4 * g + 1)
                    nc.gpsimd.tensor_tensor(yr[:, 1, :], yr[:, 0, :], neg_half[:, :], ALU.pow).then_inc(yr_d, 1)
                    wait(pool, yr_d, 4 * g + 2)
                    nc.gpsimd.tensor_tensor(yr[:, 2, :], ymv[:, :, 0], yr[:, 1, :], ALU.mult).then_inc(yr_d, 1)
                    wait_apart(pool, yr_d, 4 * g + 3)
                    nc.gpsimd.tensor_scalar(yr[:, 3, :], yr[:, 2, :], -1.0, 0.0, ALU.mult, ALU.add).then_inc(yr_d, 1)
                    wait_apart(pool, yr_d, 4 * g + 4)
                    for t in (0, 1):
                        nc.gpsimd.tensor_scalar(y_s[:, t, :], y_s[:, t, :], yr[:, 1, t:t + 1], yr[:, 3, t:t + 1],
                                                ALU.mult, ALU.add).then_inc(yhat_d, 1)

            steps(pool, body)

        @block.scalar
        def _(act):
            act.dma_start(cond[:, :, :], cond_t.rearrange("(c p) b -> p c b", p=P)).then_inc(c_in, 16)
            act.dma_start(w_e[:, :, :], w_emb.rearrange("(c p) n -> p c n", p=P)).then_inc(c_in, 16)
            act.wait_ge(c_in, 32)
            nc.scalar.activation(tanh_c[:, :, :], cond[:, :, :], ACT.Tanh, scale=0.5).then_inc(tanh_c_ready, 1)
            act.wait_ge(n_ready, 2)
            act.dma_start(n_row[0:1, :].bitcast(fp32).rearrange("o (b s) -> o b s", s=SEQ),
                          n_hi[:, :].bitcast(fp32)).then_inc(n_rows_in, 16)
            act.dma_start(n_row[1:2, :].bitcast(fp32).rearrange("o (b s) -> o b s", s=SEQ),
                          n_lo[:, :].bitcast(fp32)).then_inc(n_rows_in, 16)

            def v_tile(i, par, t):
                wait(act, qv_d, 4 * i + t + 1)
                if t == 0:
                    wait(act, att_d, i - 1)
                nc.scalar.activation(v_s[:, par, t, :, 0:DH],
                                     bqv[t][:, D:2 * D].rearrange("p (h d) -> p h d", d=DH), ACT.Copy,
                                     scale=mask_c[:, i * T + t:i * T + t + 1] if isinstance(i, int)
                                     else mask_c[:, bass.ds(i * T + t, 1)]).then_inc(v_d, 1)

            def kv_blocks(g, e):
                wait(act, rk_d, 2 * g + e + 1)
                if e == 0:
                    wait(act, y_d, 4 * g)
                for h in range(HC):
                    rows = slice(h * DH, h * DH + DH)
                    nc.scalar.activation(
                        kv[rows, e:GB:2, :, h * AW:h * AW + AW],
                        be[e][rows, 0:GB // 2 * C * AW].rearrange("p (b c n) -> p b c n", c=C, n=AW),
                        ACT.Copy).then_inc(kv_d, 1)

            def body(i, par, N, F, B, O):
                if F:
                    for c in range(C):
                        wait(act, xt_d, 2 * i + c + 1)
                        wait(act, qv_d, 4 * i)
                        nc.scalar.activation(xt_hi[:, c, :], bt[c][:, :], ACT.Copy).then_inc(hi_d, 1)
                if B:
                    g = i - 1
                    for e in range(2):
                        wait(act, ekt_d, 2 * g + e + 1)
                        wait(act, att_d, g)
                        nc.scalar.activation(e_k[:, 2 * e:2 * e + 2, :].rearrange("p t d -> p (t d)"), be[e][:, :],
                                             ACT.Copy).then_inc(ek_d, 1)
                if O:
                    g = i - 2
                    for c in range(C):
                        wait(act, z_d, 2 * g + c + 1)
                        wait(act, h_d, 2 * g)
                        nc.scalar.activation(th[:, c, :], z_s[:, c, :], ACT.Tanh, scale=0.5).then_inc(th_d, 1)
                if F:
                    for c in range(C):
                        wait(act, ksub_d, 2 * i + c + 1)
                        nc.scalar.activation(k_t[:, par, c, :], k_t[:, par, c, :], ACT.Exp).then_inc(kexp_d, 1)
                if B:
                    kv_blocks(i - 1, 0)
                    kv_blocks(i - 1, 1)
                if F:
                    v_tile(i, par, 0)
                    v_tile(i, par, 1)
                if O:
                    g = i - 2
                    for c in range(C):
                        wait(act, h_d, 2 * g + c + 1)
                        wait(act, o_d, 2 * g)
                        nc.scalar.activation(h_hi[:, c, :], h_s[:, c, :], ACT.Copy).then_inc(hhi_d, 1)
                if N:
                    g = i + 1
                    wait(act, xr_d, 4 * g + 4)
                    wait(act, xt_d, 2 * g - 2)
                    for t in range(T):
                        nc.scalar.activation(xhat[:, 1 - par, t, :],
                                             group_of(x_all, g)[:, :, t * D:t * D + D].rearrange("p g n -> p (g n)"),
                                             ACT.Identity, scale=xr[:, 1, t:t + 1],
                                             bias=xr[:, 3, t:t + 1]).then_inc(xhat_d, 1)
                if F:
                    v_tile(i, par, 2)
                    v_tile(i, par, 3)
                if B:
                    g = i - 1
                    wait(act, yr_d, 4 * g + 4)
                    for t in (2, 3):
                        nc.scalar.activation(y_s[:, t, :], y_s[:, t, :], ACT.Identity, scale=yr[:, 1, t:t + 1],
                                             bias=yr[:, 3, t:t + 1]).then_inc(yhat_a_d, 1)
                if F:
                    for e in range(2):
                        wait(act, qsub_d, 4 * i + 2 * e + 2)
                        q2 = q_s[:, par, 2 * e:2 * e + 2, :].rearrange("p t d -> p (t d)")
                        nc.scalar.activation(q2, q2, ACT.Exp).then_inc(qexp_d, 1)

            act.wait_ge(m_in, 160)
            steps(act, body)

        @block.vector
        def _(dve):
            done = [0]

            def link(ins):
                done[0] += 1
                ins.then_inc(setup_v, 1)
                dve.wait_ge(setup_v, done[0])

            def x_stats(g, parity):
                first = isinstance(g, int)
                wait(dve, x_in[parity], 16 * (g // 2 + 1) if first else 8 * (g - parity) + 16)
                wait(dve, xr_d, 4 * g)
                for t in range(T):
                    nc.vector.bn_stats(xstat[:, t, :], group_of(x_all, g)[:, :, t * D:t * D + D]
                                       .rearrange("p g n -> p (g n)")).then_inc(xstat_d, 1)
                for t in range(T):
                    wait_apart(dve, xstat_d, 4 * g + t + 1)
                    nc.vector.bn_aggr(xmv[:, t, :], xstat[:, t, :]).then_inc(xmv_d, 1)

            def setup():
                dve.wait_ge(m_in, 160)
                dve.wait_ge(pool_init, 6)
                link(nc.vector.tensor_tensor(lnb[:, :], lnb[:, :], lnw[:, :], ALU.subtract))
                link(nc.vector.memset(fold[:, :, :], 1.0))
                for c in range(C):
                    nc.vector.tensor_scalar(fold[:, c, :], fold[:, c, :], lnb[:, c:c + 1], 1.0 / D,
                                            ALU.mult, ALU.mult).then_inc(fold_ready, 1)
                link(nc.vector.tensor_scalar(mask_r[:, :], mask_r[:, :], -1.0, 1.0, ALU.mult, ALU.add))
                link(nc.vector.tensor_scalar(mask_r[:, :], mask_r[:, :], -1000000.0, None, ALU.mult))
                nc.vector.tensor_copy(n_hi[:, :], mask_r[:, :]).then_inc(n_ready, 1)
                dve.wait_ge(n_ready, 1)
                nc.vector.tensor_tensor(n_lo[:, :], mask_r[:, :], n_hi[:, :].bitcast(fp32),
                                        ALU.subtract).then_inc(n_ready, 1)
                dve.wait_ge(w_in, 80)
                dve.wait_ge(beta_done, 1)
                for c in range(C):
                    link(nc.vector.scalar_tensor_tensor(w_qv[:, c, :], w_qv[:, c, :], lnw[:, c:c + 1], bv_[0][:, :],
                                                        ALU.mult, ALU.add))
                    link(nc.vector.scalar_tensor_tensor(w_k[:, c, :], w_k[:, c, :], lnw[:, c:c + 1],
                                                        bk_[0][:, 0:D], ALU.mult, ALU.add))
                link(nc.vector.tensor_scalar(w_o, w_o, 0.5, None, ALU.mult))
                for w, hi, lo in ((w_qv[:, :, :], w_qv_hi, w_qv_lo), (w_k, w_k_hi, w_k_lo), (w_o, w_o_hi, w_o_lo)):
                    link(nc.vector.tensor_copy(hi[:, :, :], w))
                    nc.vector.tensor_tensor(lo[:, :, :], w, hi[:, :, :].bitcast(fp32),
                                            ALU.subtract).then_inc(weights_ready, 1)
                dve.wait_ge(tanh_c_ready, 1)
                nc.vector.scalar_tensor_tensor(tanh_c[:, :, :], tanh_c[:, :, :], 1.0, cond[:, :, :],
                                               ALU.add, ALU.mult).then_inc(silu_c_ready, 1)
                dve.wait_ge(emb_done, 1)
                for j in range(2 * C):
                    last = nc.vector.tensor_scalar(emb[:, j, :], bk_[1][:, j * BATCH:(j + 1) * BATCH], 0.5,
                                                   b_e[:, j:j + 1], ALU.mult, ALU.add)
                link(last)
                link(nc.vector.tensor_scalar(emb[:, 0:C, :], emb[:, 0:C, :], 1.0, None, ALU.add))
                for c in range(C):
                    nc.vector.tensor_scalar(mod_scale[:, c, :], emb[:, c, :], ln2w[:, c:c + 1], None,
                                            ALU.mult)
                    nc.vector.scalar_tensor_tensor(mod_shift[:, c, :], emb[:, c, :], ln2b[:, c:c + 1],
                                                   emb[:, C + c, :], ALU.mult, ALU.add).then_inc(mod_ready, 1)

            def q_tiles(i, par, tiles):
                q = [b[:, 0:D].rearrange("p (h d) -> p h d", d=DH) for b in bqv]
                for t in tiles:
                    wait(dve, v_d, 4 * i + t + 1)
                    wait(dve, qsub_d, 4 * i + t - 3)
                    nc.vector.tensor_reduce(out=qmax[:, t, :], in_=q[t], axis=AX.X, op=ALU.max).then_inc(qmax_d, 1)
                for t in tiles:
                    if t == 0:
                        wait(dve, eqt_d, 2 * i - 2)
                    wait(dve, qmax_d, 4 * i + t + 1)
                    nc.vector.tensor_tensor(q_s[:, par, t, :].rearrange("p (h d) -> p h d", d=DH), q[t],
                                            qmax[:, t, :].unsqueeze(2).broadcast_to([P, HEADS, DH]),
                                            ALU.subtract).then_inc(qsub_d, 1)

            def body(i, par, N, F, B, O):
                if O:
                    g = i - 2
                    for c in range(C):
                        wait(dve, yt_d, 2 * g + c + 1)
                        wait(dve, h_d, 2 * g)
                        nc.vector.tensor_tensor(
                            z_s[:, c, :].rearrange("p (b s) -> p b s", s=SEQ),
                            be[c][:, :].rearrange("p (b s) -> p b s", s=SEQ),
                            mod_scale[:, c, span(g, GB)].unsqueeze(2).broadcast_to([P, GB, SEQ]),
                            ALU.mult).then_inc(zs_d, 1)
                if F:
                    for c in range(C):
                        wait(dve, hi_d, 2 * i + c + 1)
                        nc.vector.tensor_tensor(xt_lo[:, c, :], bt[c][:, :], xt_hi[:, c, :].bitcast(fp32),
                                                ALU.subtract).then_inc(lo_d, 1)
                if N:
                    x_stats(i + 1, 1 - par)
                if F:
                    for c in range(C):
                        wait(dve, k_d, 2 * i + c + 1)
                        wait(dve, ksub_d, 2 * i + c - 1)
                        kk = bk_[c][:, :].rearrange("p (b s) -> p b s", s=SEQ)
                        nc.vector.tensor_reduce(out=kmax[:, c, :], in_=kk, axis=AX.X, op=ALU.max).then_inc(kmax_d, 1)
                        wait(dve, kmax_d, 2 * i + c + 1)
                        if c == 0:
                            wait(dve, ekt_d, 2 * i - 2)
                        nc.vector.tensor_tensor(k_t[:, par, c, :].rearrange("p (b s) -> p b s", s=SEQ), kk,
                                                kmax[:, c, :].unsqueeze(2).broadcast_to([P, GB, SEQ]),
                                                ALU.subtract).then_inc(ksub_d, 1)
                if O:
                    g = i - 2
                    for c in range(C):
                        wait(dve, th_d, 2 * g + c + 1)
                        wait(dve, hlo_d, 2 * g)
                        nc.vector.scalar_tensor_tensor(h_s[:, c, :], th[:, c, :], 1.0, z_s[:, c, :],
                                                       ALU.add, ALU.mult).then_inc(h_d, 1)
                if B:
                    g = i - 1
                    wait(dve, att_d, g + 1)
                    wait(dve, qt_d, 2 * g)
                    for e in range(2):
                        sums = be[e][:, 0:GB // 2 * C * AW].rearrange("p (b c n) -> p b c n", c=C, n=AW)
                        nc.vector.reciprocal(rk[:, e, :, :], sums[:, :, :, DH]).then_inc(rk_d, 1)
                if B:
                    g = i - 1
                    wait(dve, rk_d, 2 * g + 2)
                    wait(dve, y_d, 4 * g)
                    for c in range(C):
                        wait(dve, eqt_d, 2 * g + c + 1)
                        nc.vector.tensor_tensor(
                            q_t[:, c, :].rearrange("p (b e s) -> p b e s", e=2, s=SEQ),
                            bt[c][:, :].rearrange("p (b e s) -> p b e s", e=2, s=SEQ),
                            rk[:, :, :, c].rearrange("p e b -> p b e").unsqueeze(3)
                            .broadcast_to([P, GB // 2, 2, SEQ]), ALU.mult).then_inc(qt_d, 1)
                if F:
                    q_tiles(i, par, (0, 1))
                if B:
                    g = i - 1
                    y_of = [b[:, 0:C * HC * AW].rearrange("p (h n) -> p h n", n=AW) for b in be + bt]

                    def y_norm(t):
                        wait(dve, rq_d, 4 * g + t + 1)
                        nc.vector.tensor_tensor(y_s[:, t, :].rearrange("p (h d) -> p h d", d=DH),
                                                y_of[t][:, :, 0:DH],
                                                rq[:, t, :].unsqueeze(2).broadcast_to([P, HEADS, DH]),
                                                ALU.mult).then_inc(ys_d, 1)

                    def y_stat(t):
                        wait(dve, ys_d, 4 * g + t + 1)
                        nc.vector.bn_stats(ystat[:, t, :], y_s[:, t, :]).then_inc(ystat_d, 1)

                    wait(dve, yt_d, 2 * g)
                    wait(dve, ys_d, 4 * g)
                    wait(dve, yr_d, 4 * g)
                    for t in range(T):
                        wait(dve, y_d, 4 * g + t + 1)
                        nc.vector.reciprocal(rq[:, t, :], y_of[t][:, :, DH]).then_inc(rq_d, 1)
                        if t > 1:
                            y_stat(t - 2)
                        if t > 0:
                            y_norm(t - 1)
                    y_stat(T - 2)
                    y_norm(T - 1)
                    y_stat(T - 1)
                    for t in range(T):
                        wait_apart(dve, ystat_d, 4 * g + t + 1)
                        nc.vector.bn_aggr(ymv[:, t, :], ystat[:, t, :]).then_inc(ymv_d, 1)
                if F:
                    q_tiles(i, par, (2, 3))
                if O:
                    g = i - 2
                    wait(dve, xb_d, g + 1)
                    for e in range(2):
                        wait(dve, o_d, 2 * g + e + 1)
                        xg = group_of(x_all, g)[:, :, 2 * e * D:2 * e * D + 2 * D].rearrange("p g n -> p (g n)")
                        nc.vector.tensor_tensor(xg, bv_[e][:, :], xg, ALU.add).then_inc(res_d, 1)

            setup()
            steps(dve, body)

        @block.tensor
        def _(pe):
            def mm(dst, lhsT, rhs, start, stop):
                return nc.tensor.matmul(dst, lhsT, rhs, start=start, stop=stop)

            pe.wait_ge(w_in, 80)
            pe.wait_ge(fold_ready, C)
            for dst, w, b0, n in ((bv_[0], w_qv, 0, 2 * D), (bk_[0], w_k, 2 * D, D)):
                for c in range(C):
                    mm(dst[:, 0:n], fold[:, c, :], w[:, c, :], c == 0, False)
                last = mm(dst[:, 0:n], inv_row[:, :], brow[:, b0:b0 + n], False, True)
            last.then_inc(beta_done, 1)
            pe.wait_ge(silu_c_ready, 1)
            pe.wait_ge(c_in, 32)
            for j in range(2 * C):
                for c in range(EC):
                    last = mm(bk_[1][:, j * BATCH:(j + 1) * BATCH], w_e[:, c, j * P:(j + 1) * P], tanh_c[:, c, :],
                              c == 0, c == EC - 1)
            last.then_inc(emb_done, 1)

            def qv_tile(i, t):
                if t < 2:
                    wait(pe, qsub_d, 4 * i + t - 3)
                    wait(pe, res_d, 2 * (i - 3) + t + 1)
                else:
                    wait(pe, ksub_d, 2 * i + t - 1)
                tok = slice(t * P, t * P + P)
                parts = [(xt_hi, w_qv_hi), (xt_hi, w_qv_lo), (xt_lo, w_qv_hi)]
                for n, (a, w) in enumerate(parts):
                    for c in range(C):
                        last = mm(bqv[t][:, :], a[:, c, tok], w[:, c, :], n + c == 0,
                                  n == len(parts) - 1 and c == C - 1)
                last.then_inc(qv_d, 1)

            def body(i, par, N, F, B, O):
                if F:
                    for c in range(C):
                        if c == 0:
                            wait(pe, xhat_d, 4 * i + 4)
                        wait(pe, ys_d, 4 * (i - 2) + c + 3)
                        for t in range(T):
                            last = nc.tensor.transpose(bt[c][:, t * P:t * P + P], xhat[:, par, t, c * P:c * P + P],
                                                       ident[:, :])
                        last.then_inc(xt_d, 1)
                if B:
                    g = i - 1
                    wait(pe, kexp_d, 2 * g + 2)
                    for e in range(2):
                        wait(pe, zs_d, 2 * (g - 1) + e + 1)
                        for t in (2 * e, 2 * e + 1):
                            for c in range(C):
                                last = nc.tensor.transpose(be[e][:, (t % 2) * D + c * P:(t % 2) * D + c * P + P],
                                                           k_t[:, 1 - par, c, t * P:t * P + P], ident[:, :])
                        last.then_inc(ekt_d, 1)
                if F:
                    for c in range(C):
                        out_c = slice(c * P, c * P + P)
                        wait_apart(pe, qsub_d, 4 * i + c - 1)
                        mm(bk_[c][:, :], ones2[:, :], n_row[:, span(i, GT)], True, False)
                        wait(pe, hi_d, 2 * i + 2)
                        for j in range(C):
                            mm(bk_[c][:, :], w_k_hi[:, j, out_c], xt_hi[:, j, :], False, False)
                            mm(bk_[c][:, :], w_k_lo[:, j, out_c], xt_hi[:, j, :], False, False)
                        wait(pe, lo_d, 2 * i + 2)
                        for j in range(C):
                            last = mm(bk_[c][:, :], w_k_hi[:, j, out_c], xt_lo[:, j, :], False, j == C - 1)
                        last.then_inc(k_d, 1)
                if B:
                    g = i - 1
                    wait(pe, qexp_d, 2 * g + 2)
                    for c in range(C):
                        wait(pe, lo_d, 2 * (g + 1) + c + 1 if F else 2 * G)
                        for t in range(T):
                            last = nc.tensor.transpose(bt[c][:, t * P:t * P + P], q_s[:, 1 - par, t, c * P:c * P + P],
                                                       ident[:, :])
                        last.then_inc(eqt_d, 1)
                if B:
                    g = i - 1
                    wait(pe, ek_d, 2 * g + 2)
                    wait_apart(pe, v_d, 4 * g + 4)
                    for b in range(GB):
                        t, e = b // 2, b % 2
                        rows = slice(e * SEQ, e * SEQ + SEQ)
                        for c in range(C):
                            col = (t * C + c) * AW
                            for h in range(HC):
                                ch = c * P + h * DH
                                last = mm(be[e][h * DH:h * DH + DH, col:col + AW], e_k[rows, t, ch:ch + DH],
                                          v_s[rows, 1 - par, t, c * HC + h, :], True, True)
                    last.then_inc(att_d, 1)
                if F:
                    qv_tile(i, 0)
                    qv_tile(i, 1)
                if B:
                    g = i - 1
                    wait(pe, kv_d, 8 * g + 8)
                    wait(pe, qt_d, 2 * g + 2)
                    for t in range(T):
                        yb = be[t] if t < 2 else bt[t - 2]
                        for c in range(C):
                            for e in range(2):
                                last = mm(yb[e * SEQ:e * SEQ + SEQ, c * HC * AW:(c + 1) * HC * AW],
                                          q_t[:, c, t * P + e * SEQ:t * P + e * SEQ + SEQ], kv[:, 2 * t + e, c, :],
                                          True, True)
                        last.then_inc(y_d, 1)
                if F:
                    qv_tile(i, 2)
                    qv_tile(i, 3)
                if O:
                    g = i - 2
                    wait(pe, hlo_d, 2 * g + 2)
                    parts = [(h_hi, w_o_hi), (h_hi, w_o_lo), (h_lo, w_o_hi)]
                    for e in range(2):
                        wait(pe, qsub_d, 4 * i + e + 1 if F else 4 * G)
                        if not F:
                            wait(pe, res_d, 2 * g + e - 1)
                        for t in (2 * e, 2 * e + 1):
                            for n, (a, w) in enumerate(parts):
                                for c in range(C):
                                    last = mm(bv_[e][:, (t % 2) * D:(t % 2) * D + D], a[:, c, t * P:t * P + P],
                                              w[:, c, :], n + c == 0, n == len(parts) - 1 and c == C - 1)
                        last.then_inc(o_d, 1)
                if B:
                    g = i - 1
                    wait(pe, yhat_d, 2 * g + 2)
                    wait(pe, yhat_a_d, 2 * g + 2)
                    for c in range(C):
                        wait(pe, ys_d, 4 * g + c + 1)
                        for t in range(T):
                            last = nc.tensor.transpose(be[c][:, t * P:t * P + P], y_s[:, t, c * P:c * P + P],
                                                       ident[:, :])
                        last.then_inc(yt_d, 1)

            pe.wait_ge(pool_init, 6)
            pe.wait_ge(n_rows_in, 32)
            pe.wait_ge(weights_ready, 3)
            steps(pe, body)


_ARGS = ["x", "cond_t", "mask_cols", "mask_rows", "ln_w", "ln_b", "wq", "bq", "wk", "bk", "wv", "bv", "w_emb",
         "b_emb", "ln2_w", "ln2_b", "w_out", "b_out"]


def kernel(x, cond_2048, mask_BxSx1_fk1, L0_cond_ln_w, L0_cond_ln_b, L0_cond_Wq, L0_cond_bq, L0_cond_Wk, L0_cond_bk,
           L0_cond_Wv, L0_cond_bv, L0_cond_W_emb, L0_cond_b_emb, L0_cond_ln2_w, L0_cond_ln2_b, L0_cond_W_out,
           L0_cond_b_out):
    import concourse.bacc as _bacc
    from concourse.bass_utils import run_bass_kernel_spmd as _run

    b, s, d = x.shape
    P = 128

    def columns(v):
        return np.ascontiguousarray(np.asarray(v).reshape(-1, P).T)

    mask = np.asarray(mask_BxSx1_fk1)
    arrays = [np.asarray(x).reshape(b * s, d), np.ascontiguousarray(np.asarray(cond_2048).T), columns(mask.reshape(-1)),
              mask.reshape(b, s), columns(L0_cond_ln_w), columns(L0_cond_ln_b), L0_cond_Wq, L0_cond_bq, L0_cond_Wk,
              L0_cond_bk, L0_cond_Wv, L0_cond_bv, L0_cond_W_emb, columns(L0_cond_b_emb), columns(L0_cond_ln2_w),
              columns(L0_cond_ln2_b), L0_cond_W_out, L0_cond_b_out]
    nc = _bacc.Bacc("TRN2", target_bir_lowering=False, num_devices=1)
    feed, args = {}, []
    for name, a in zip(_ARGS, arrays):
        a = np.ascontiguousarray(a)
        feed[f"in_{name}"] = a
        args.append(nc.dram_tensor(f"in_{name}", a.shape, mybir.dt.from_np(a.dtype), kind="ExternalInput").ap())
    out = nc.dram_tensor("out_0", (b * s, d), mybir.dt.float32, kind="ExternalOutput").ap()
    build_layer(nc, *args, out)
    r = _run(nc, [feed], core_ids=[0])
    return r.results[0]["out_0"].reshape(b, s, d)
```

```python
import numpy as np
import concourse.bass as bass
from concourse import mybir
from contextlib import ExitStack


def build_layer(nc, x, cond_t, columns_in, b_qvk, mask_rows, wq, wk, wv, w_emb, w_out, b_out, out):
    fp32 = mybir.dt.float32
    f32r = mybir.dt.float32r
    ALU = mybir.AluOpType
    ACT = mybir.ActivationFunctionType
    AX = mybir.AxisListType

    P = 128
    ROWS, D = x.shape
    BATCH, SEQ = mask_rows.shape
    HEADS = 8
    DH = D // HEADS
    C = D // P
    HC = HEADS // C
    GT = 512
    G = ROWS // GT
    T = GT // P
    GB = GT // SEQ
    E = cond_t.shape[0]
    EC = E // P
    AW = DH + 1
    EPS = 1e-5

    ctx = ExitStack()
    with ctx:
        def sb(name, shape, dt=fp32):
            return ctx.enter_context(nc.sbuf_tensor(name, shape, dt))

        def sem(name):
            return ctx.enter_context(nc.semaphore(name))

        x_all = sb("x_all", [P, G, T * D])
        w_qv_hi = sb("w_qv_hi", [P, C, 2 * D], f32r)
        w_qv_lo = sb("w_qv_lo", [P, C, 2 * D], f32r)
        w_k_hi = sb("w_k_hi", [P, C, D], f32r)
        w_k_lo = sb("w_k_lo", [P, C, D], f32r)
        w_o_hi = sb("w_o_hi", [P, C, D], f32r)
        w_o_lo = sb("w_o_lo", [P, C, D], f32r)
        bo_all = sb("bo_all", [P, D])
        ident = sb("ident", [P, P])
        mod_scale = sb("mod_scale", [P, C, BATCH])
        mod_shift = sb("mod_shift", [P, C, BATCH])
        n_row = sb("n_row", [2, ROWS], f32r)
        ones2 = sb("ones2", [2, P], f32r)
        neg_half = sb("neg_half", [P, T])

        small = sb("small", [P, 6 * C + ROWS // P])
        lnw, lnb, ln2w, ln2b = (small[:, n * C:n * C + C] for n in range(4))
        b_e = small[:, 4 * C:6 * C]
        mask_c = small[:, 6 * C:]

        emb = sb("emb", [P, 2 * C, BATCH])
        brow = sb("brow", [1, 3 * D])
        fold = sb("fold", [P, C, P])
        inv_row = sb("inv_row", [1, P])
        mask_r = sb("mask_r", [P, SEQ])
        n_hi = sb("n_hi", [P, SEQ], f32r)
        n_lo = sb("n_lo", [P, SEQ], f32r)

        xstat = sb("xstat", [P, T, 6])
        xmv = sb("xmv", [P, T, 2])
        xr = sb("xr", [P, 4, T])
        xhat = sb("xhat", [P, 2, T, D])
        xt_hi = sb("xt_hi", [P, C, GT], f32r)
        xt_lo = sb("xt_lo", [P, C, GT], f32r)
        kmax = sb("kmax", [P, C, GB])
        k_t = sb("k_t", [P, 2, C, GT])
        qmax = sb("qmax", [P, T, HEADS])
        q_s = sb("q_s", [P, 2, T, D])
        v_s = sb("v_s", [P, 2, T, HEADS, AW])
        e_k = sb("e_k", [P, T, D])
        kv = sb("kv", [P, GB, C, HC * AW])
        rk = sb("rk", [P, 2, GB // 2, C])
        q_t = sb("q_t", [P, C, GT])
        rq = sb("rq", [P, T, HEADS])
        y_s = sb("y_s", [P, T, D])
        ystat = sb("ystat", [P, T, 6])
        ymv = sb("ymv", [P, T, 2])
        yr = sb("yr", [P, 4, T])
        z_s = sb("z_s", [P, C, GT])
        th = sb("th", [P, C, GT])
        h_s = sb("h_s", [P, C, GT])
        h_hi = sb("h_hi", [P, C, GT], f32r)
        h_lo = sb("h_lo", [P, C, GT], f32r)

        w_qv = q_t
        w_o = y_s[:, 0:C, :]
        w_k = y_s[:, C:2 * C, :]
        w_e = [z_s, h_s]
        cond = th[:, 0, :].rearrange("p (c b) -> p c b", c=EC)
        tanh_c = th[:, 1, :].rearrange("p (c b) -> p c b", c=EC)

        def bank(name):
            return ctx.enter_context(nc.psum_tensor(name, [P, 512], fp32))
        bt = [bank("bt0"), bank("bt1")]
        be = [bank("be0"), bank("be1")]
        bk_ = [bank("bk0"), bank("bk1")]
        bv_ = [bank("bv0"), bank("bv1")]
        bqv = bv_ + bk_

        small_in = sem("small_in")
        brow_in = sem("brow_in")
        mask_in = sem("mask_in")
        wk_in = sem("wk_in")
        wqv_in = sem("wqv_in")
        wo_in = sem("wo_in")
        bo_in = sem("bo_in")
        cond_in = sem("cond_in")
        we_in = sem("we_in")
        n_rows_in = sem("n_rows_in")
        x_in = [sem("x_in0"), sem("x_in1")]
        stored = sem("stored")
        pool_init = sem("pool_init")
        id_zero = sem("id_zero")
        fold_ready = sem("fold_ready")
        beta_done = sem("beta_done")
        tanh_c_ready = sem("tanh_c_ready")
        silu_c_ready = sem("silu_c_ready")
        emb_done = sem("emb_done")
        emb_out = sem("emb_out")
        n_ready = sem("n_ready")
        setup_v = sem("setup_v")
        weights_ready = sem("weights_ready")
        mod_ready = sem("mod_ready")
        xstat_d = sem("xstat_d")
        xmv_d = sem("xmv_d")
        xr_d = sem("xr_d")
        xhat_d = sem("xhat_d")
        xt_d = sem("xt_d")
        hi_d = sem("hi_d")
        lo_d = sem("lo_d")
        k_d = sem("k_d")
        kmax_d = sem("kmax_d")
        ksub_d = sem("ksub_d")
        kexp_d = sem("kexp_d")
        qv_d = sem("qv_d")
        v_d = sem("v_d")
        qmax_d = sem("qmax_d")
        qsub_d = sem("qsub_d")
        qexp_d = sem("qexp_d")
        ekt_d = sem("ekt_d")
        ek_d = sem("ek_d")
        att_d = sem("att_d")
        rk_d = sem("rk_d")
        kv_d = sem("kv_d")
        kv_v_d = sem("kv_v_d")
        eqt_d = sem("eqt_d")
        qt_d = sem("qt_d")
        y_d = sem("y_d")
        rq_d = sem("rq_d")
        ys_d = sem("ys_d")
        ystat_d = sem("ystat_d")
        ymv_d = sem("ymv_d")
        yve_d = sem("yve_d")
        yr_d = sem("yr_d")
        yhat_d = sem("yhat_d")
        yt_d = sem("yt_d")
        zs_d = sem("zs_d")
        z_d = sem("z_d")
        th_d = sem("th_d")
        h_d = sem("h_d")
        hhi_d = sem("hhi_d")
        hlo_d = sem("hlo_d")
        xb_d = sem("xb_d")
        o_d = sem("o_d")
        res_d = sem("res_d")

        block = ctx.enter_context(nc.Block())

        def wait(eng, s, n):
            if isinstance(n, int) and n <= 0:
                return
            eng.wait_ge(s, n)

        def wait_apart(eng, s, n):
            wait(eng, s, n)
            if not isinstance(n, int):
                eng.nop(nofuse=True)

        def steps(eng, body, after_first=None):
            def at(i):
                body(i, i % 2, i + 1 < G, 0 <= i < G, 0 <= i - 1 < G, 0 <= i - 2 < G)
            at(-1)
            if after_first:
                after_first()
            for i in (0, 1, 2):
                at(i)
            with eng.Fori(1, G // 2 - 1) as turn:
                body(2 * turn + 1, 1, True, True, True, True)
                body(2 * turn + 2, 0, True, True, True, True)
            for i in range(G - 1, G + 2):
                at(i)

        def last_step(i):
            return isinstance(i, int) and i == G + 1

        def last_y(i):
            return isinstance(i, int) and i == G

        def shift(eng, g, c):
            z = z_s[:, c, :].rearrange("p (b s) -> p b s", s=SEQ)
            return eng.tensor_tensor(z, z, mod_shift[:, c, span(g, GB)].unsqueeze(2).broadcast_to([P, GB, SEQ]),
                                     ALU.add)

        def h_low(eng, c):
            return eng.tensor_tensor(h_lo[:, c, :], h_s[:, c, :], h_hi[:, c, :].bitcast(fp32), ALU.subtract)

        x_h = x.rearrange("(g t p) d -> g p t d", t=T, p=P)
        o_h = out.rearrange("(g t p) d -> g p t d", t=T, p=P)

        def group_of(tensor, g):
            return tensor[:, g:g + 1, :] if isinstance(g, int) else tensor[:, bass.ds(g, 1), :]

        def span(g, n):
            return slice(g * n, g * n + n) if isinstance(g, int) else bass.ds(g * n, n)

        @block.sync
        def _(sp):
            def load_x(g, parity):
                sp.dma_start(group_of(x_all, g).rearrange("p g (t d) -> p (g t) d", t=T),
                             x_h[span(g, 1)].rearrange("g p t d -> p (g t) d")).then_inc(x_in[parity], 16)

            sp.dma_start(w_k, wk.rearrange("(c p) n -> p c n", p=P)).then_inc(wk_in, 16)
            load_x(0, 0)
            sp.dma_start(w_qv[:, :, 0:D], wq.rearrange("(c p) n -> p c n", p=P)).then_inc(wqv_in, 16)
            sp.dma_start(w_qv[:, :, D:2 * D], wv.rearrange("(c p) n -> p c n", p=P)).then_inc(wqv_in, 16)
            sp.dma_start(w_o, w_out.rearrange("(c p) n -> p c n", p=P)).then_inc(wo_in, 16)
            load_x(1, 1)
            sp.dma_start(bo_all[:, :], b_out[None, :].broadcast_to([P, D])).then_inc(bo_in, 16)

            def store(g):
                wait(sp, res_d, 2 * g + 2)
                sp.dma_start(o_h[span(g, 1)].rearrange("g p t d -> p (g t) d"),
                             group_of(x_all, g).rearrange("p g (t d) -> p (g t) d", t=T)).then_inc(stored, 16)

            def body(i, par, N, F, B, O):
                if N and not (isinstance(i, int) and i < 1):
                    wait(sp, xstat_d, 4 * i)
                    load_x(i + 1, 1 - par)
                if O and not (isinstance(i, int) and i < 3):
                    store(i - 3)

            steps(sp, body)
            for e in range(2):
                sp.wait_ge(res_d, 2 * (G - 1) + e + 1)
                sp.dma_start(o_h[G - 1][:, 2 * e:2 * e + 2, :],
                             x_all[:, G - 1, 2 * e * D:(2 * e + 2) * D].rearrange("p (t d) -> p t d", d=D)
                             ).then_inc(stored, 16)
            sp.wait_ge(stored, 16 * (G + 1))

        @block.gpsimd
        def _(pool):
            pool.memset(ident[:, :], 0.0).then_inc(id_zero, 1)
            pool.memset(neg_half[:, :], -0.5).then_inc(pool_init, 1)
            pool.wait_ge(id_zero, 1)
            pool.affine_select(out=ident[:, :], in_=ident[:, :], compare_op=ALU.not_equal, fill=1.0, base=0,
                               pattern=[[-1, P]], channel_multiplier=1).then_inc(pool_init, 1)
            pool.memset(inv_row[:, :], 1.0 / D).then_inc(pool_init, 1)
            pool.memset(ones2[:, :].bitcast(fp32), 1.0).then_inc(pool_init, 1)
            pool.memset(v_s[:, :, :, :, DH:AW], 1.0).then_inc(pool_init, 1)
            pool.memset(kv[:, :, :, :], 0.0).then_inc(pool_init, 1)

            def body(i, par, N, F, B, O):
                if O and not last_step(i):
                    g = i - 2
                    if isinstance(g, int) and g == 0:
                        pool.wait_ge(mod_ready, C)
                    for c in range(C):
                        wait(pool, zs_d, 2 * g + c + 1)
                        shift(nc.gpsimd, g, c).then_inc(z_d, 1)
                if N:
                    g = i + 1
                    if isinstance(g, int) and g == 0:
                        pool.wait_ge(pool_init, 1)
                    wait(pool, xhat_d, 4 * g)
                    wait_apart(pool, xmv_d, 4 * g + 4)
                    nc.gpsimd.tensor_scalar(xr[:, 0, :], xmv[:, :, 1], 1.0, EPS, ALU.mult, ALU.add).then_inc(xr_d, 1)
                    wait(pool, xr_d, 4 * g + 1)
                    nc.gpsimd.tensor_tensor(xr[:, 1, :], xr[:, 0, :], neg_half[:, :], ALU.pow).then_inc(xr_d, 1)
                    wait(pool, xr_d, 4 * g + 2)
                    nc.gpsimd.tensor_tensor(xr[:, 2, :], xmv[:, :, 0], xr[:, 1, :], ALU.mult).then_inc(xr_d, 1)
                    wait_apart(pool, xr_d, 4 * g + 3)
                    nc.gpsimd.tensor_scalar(xr[:, 3, :], xr[:, 2, :], -1.0, 1.0, ALU.mult, ALU.add).then_inc(xr_d, 1)
                if F:
                    g = i
                    if isinstance(g, int) and g == 0:
                        pool.wait_ge(bo_in, 16)
                    wait(pool, xhat_d, 4 * g + 4)
                    xg = group_of(x_all, g).rearrange("p g (t d) -> p (g t) d", t=T)
                    nc.gpsimd.tensor_tensor(xg, xg, bo_all[:, :].unsqueeze(1).broadcast_to([P, T, D]),
                                            ALU.add).then_inc(xb_d, 1)
                if O and not last_step(i):
                    g = i - 2
                    for c in range(C):
                        wait(pool, hhi_d, 2 * g + c + 1)
                        wait(pool, o_d, 2 * g)
                        h_low(nc.gpsimd, c).then_inc(hlo_d, 1)
                if B:
                    g = i - 1
                    wait(pool, yhat_d, 4 * g)
                    wait(pool, yve_d, 2 * g + 2)
                    nc.gpsimd.tensor_tensor(yr[:, 1, :], yr[:, 0, :], neg_half[:, :], ALU.pow).then_inc(yr_d, 1)
                    wait(pool, yr_d, 2 * g + 1)
                    nc.gpsimd.tensor_tensor(yr[:, 3, :], yr[:, 2, :], yr[:, 1, :], ALU.mult).then_inc(yr_d, 1)
                    wait_apart(pool, yr_d, 2 * g + 2)
                    for t in range(T) if not last_y(i) else (0, 1):
                        nc.gpsimd.tensor_scalar(y_s[:, t, :], y_s[:, t, :], yr[:, 1, t:t + 1], yr[:, 3, t:t + 1],
                                                ALU.mult, ALU.add).then_inc(yhat_d, 1)

            steps(pool, body)

        @block.scalar
        def _(act):
            act.dma_start(small[:, :], columns_in).then_inc(small_in, 16)
            act.dma_start(brow[:, :], b_qvk[None, :]).then_inc(brow_in, 16)
            act.dma_start(mask_r[:, :], mask_rows).then_inc(mask_in, 16)
            act.dma_start(cond[:, :, :], cond_t.rearrange("(c p) b -> p c b", p=P)).then_inc(cond_in, 16)
            for n in range(2):
                act.dma_start(w_e[n][:, :, :], w_emb[n * 2 * P:(n + 1) * 2 * P, :]
                              .rearrange("(c p) n -> p c n", p=P)).then_inc(we_in, 16)
            act.wait_ge(n_ready, 2)
            act.dma_start(n_row[0:1, :].bitcast(fp32).rearrange("o (b s) -> o b s", s=SEQ),
                          n_hi[:, :].bitcast(fp32)).then_inc(n_rows_in, 16)
            act.dma_start(n_row[1:2, :].bitcast(fp32).rearrange("o (b s) -> o b s", s=SEQ),
                          n_lo[:, :].bitcast(fp32)).then_inc(n_rows_in, 16)
            act.wait_ge(cond_in, 16)
            nc.scalar.activation(tanh_c[:, :, :], cond[:, :, :], ACT.Tanh, scale=0.5).then_inc(tanh_c_ready, 1)

            def v_tile(i, par, t):
                wait(act, qv_d, 4 * i + t + 1)
                if t == 0:
                    wait(act, att_d, i - 1)
                nc.scalar.activation(v_s[:, par, t, :, 0:DH],
                                     bqv[t][:, D:2 * D].rearrange("p (h d) -> p h d", d=DH), ACT.Copy,
                                     scale=mask_c[:, i * T + t:i * T + t + 1] if isinstance(i, int)
                                     else mask_c[:, bass.ds(i * T + t, 1)]).then_inc(v_d, 1)

            def kv_blocks(g, e):
                wait(act, rk_d, 2 * g + e + 1)
                if e == 1:
                    wait(act, kv_v_d, g + 1)
                if e == 0:
                    wait(act, y_d, 4 * g)
                for h in range(HC - e):
                    rows = slice(h * DH, h * DH + DH)
                    nc.scalar.activation(
                        kv[rows, e:GB:2, :, h * AW:h * AW + AW],
                        be[e][rows, 0:GB // 2 * C * AW].rearrange("p (b c n) -> p b c n", c=C, n=AW),
                        ACT.Copy).then_inc(kv_d, 1)

            def body(i, par, N, F, B, O):
                if F:
                    for c in range(C):
                        wait(act, xt_d, 2 * i + c + 1)
                        wait(act, qv_d, 4 * i)
                        nc.scalar.activation(xt_hi[:, c, :], bt[c][:, :], ACT.Copy).then_inc(hi_d, 1)
                if B:
                    g = i - 1
                    for e in range(2):
                        wait(act, ekt_d, 2 * g + e + 1)
                        wait(act, att_d, g)
                        nc.scalar.activation(e_k[:, 2 * e:2 * e + 2, :].rearrange("p t d -> p (t d)"), be[e][:, :],
                                             ACT.Copy).then_inc(ek_d, 1)
                if B:
                    g = i - 1
                    for e in range(2):
                        wait(act, qsub_d, 4 * g + 2 * e + 2)
                        q2 = q_s[:, 1 - par, 2 * e:2 * e + 2, :].rearrange("p t d -> p (t d)")
                        nc.scalar.activation(q2, q2, ACT.Exp).then_inc(qexp_d, 1)
                if F:
                    for c in range(C):
                        wait(act, ksub_d, 2 * i + c + 1)
                        nc.scalar.activation(k_t[:, par, c, :], k_t[:, par, c, :], ACT.Exp).then_inc(kexp_d, 1)
                if O:
                    g = i - 2
                    for c in range(C):
                        wait(act, z_d, 2 * g + c + 1)
                        wait(act, h_d, 2 * g)
                        nc.scalar.activation(th[:, c, :], z_s[:, c, :], ACT.Tanh, scale=0.5).then_inc(th_d, 1)
                if B:
                    kv_blocks(i - 1, 0)
                    kv_blocks(i - 1, 1)
                if F:
                    if isinstance(i, int) and i == 0:
                        act.wait_ge(emb_done, 1)
                        for j in range(2 * C):
                            nc.scalar.activation(emb[:, j, :], be[1][:, j * BATCH:(j + 1) * BATCH], ACT.Identity,
                                                 scale=0.5, bias=b_e[:, j:j + 1]).then_inc(emb_out, 1)
                    v_tile(i, par, 0)
                    v_tile(i, par, 1)
                if O:
                    g = i - 2
                    for c in range(C):
                        wait(act, h_d, 2 * g + c + 1)
                        wait(act, o_d, 2 * g)
                        nc.scalar.activation(h_hi[:, c, :], h_s[:, c, :], ACT.Copy).then_inc(hhi_d, 1)
                if N:
                    g = i + 1
                    wait(act, xr_d, 4 * g + 4)
                    wait(act, xt_d, 2 * g - 2)
                    for t in range(T):
                        nc.scalar.activation(xhat[:, 1 - par, t, :],
                                             group_of(x_all, g)[:, :, t * D:t * D + D].rearrange("p g n -> p (g n)"),
                                             ACT.Identity, scale=xr[:, 1, t:t + 1],
                                             bias=xr[:, 3, t:t + 1]).then_inc(xhat_d, 1)
                if F:
                    v_tile(i, par, 2)
                    v_tile(i, par, 3)
                if B and last_y(i):
                    g = i - 1
                    wait(act, yr_d, 2 * g + 2)
                    for t in (2, 3):
                        nc.scalar.activation(y_s[:, t, :], y_s[:, t, :], ACT.Identity, scale=yr[:, 1, t:t + 1],
                                             bias=yr[:, 3, t:t + 1]).then_inc(yhat_d, 1)

            act.wait_ge(small_in, 16)
            steps(act, body)

        @block.vector
        def _(dve):
            done = [0]

            def link(ins):
                done[0] += 1
                ins.then_inc(setup_v, 1)
                dve.wait_ge(setup_v, done[0])

            def x_stats(g, parity):
                first = isinstance(g, int)
                wait(dve, x_in[parity], 16 * (g // 2 + 1) if first else 8 * (g - parity) + 16)
                wait(dve, xr_d, 4 * g)
                for t in range(T):
                    nc.vector.bn_stats(xstat[:, t, :], group_of(x_all, g)[:, :, t * D:t * D + D]
                                       .rearrange("p g n -> p (g n)")).then_inc(xstat_d, 1)
                for t in range(T):
                    wait_apart(dve, xstat_d, 4 * g + t + 1)
                    nc.vector.bn_aggr(xmv[:, t, :], xstat[:, t, :]).then_inc(xmv_d, 1)

            def fold_and_mask():
                dve.wait_ge(small_in, 16)
                link(nc.vector.tensor_tensor(lnb, lnb, lnw, ALU.subtract))
                link(nc.vector.memset(fold[:, :, :], 1.0))
                for c in range(C):
                    nc.vector.tensor_scalar(fold[:, c, :], fold[:, c, :], lnb[:, c:c + 1], 1.0 / D,
                                            ALU.mult, ALU.mult).then_inc(fold_ready, 1)
                dve.wait_ge(mask_in, 16)
                link(nc.vector.tensor_scalar(mask_r[:, :], mask_r[:, :], -1.0, 1.0, ALU.mult, ALU.add))
                link(nc.vector.tensor_scalar(mask_r[:, :], mask_r[:, :], -1000000.0, None, ALU.mult))
                nc.vector.tensor_copy(n_hi[:, :], mask_r[:, :]).then_inc(n_ready, 1)
                dve.wait_ge(n_ready, 1)
                nc.vector.tensor_tensor(n_lo[:, :], mask_r[:, :], n_hi[:, :].bitcast(fp32),
                                        ALU.subtract).then_inc(n_ready, 1)

            def split(w, hi, lo):
                link(nc.vector.tensor_copy(hi[:, :, :], w))
                nc.vector.tensor_tensor(lo[:, :, :], w, hi[:, :, :].bitcast(fp32),
                                        ALU.subtract).then_inc(weights_ready, 1)

            def weights_k():
                dve.wait_ge(wk_in, 16)
                dve.wait_ge(beta_done, 1)
                for c in range(C):
                    last = nc.vector.scalar_tensor_tensor(w_k[:, c, :], w_k[:, c, :], lnw[:, c:c + 1],
                                                          bk_[0][:, 0:D], ALU.mult, ALU.add)
                link(last)
                split(w_k, w_k_hi, w_k_lo)
                dve.wait_ge(tanh_c_ready, 1)
                nc.vector.scalar_tensor_tensor(tanh_c[:, :, :], tanh_c[:, :, :], 1.0, cond[:, :, :],
                                               ALU.add, ALU.mult).then_inc(silu_c_ready, 1)

            def weights_qv():
                dve.wait_ge(wqv_in, 32)
                dve.wait_ge(beta_done, 2)
                for c in range(C):
                    last = nc.vector.scalar_tensor_tensor(w_qv[:, c, :], w_qv[:, c, :], lnw[:, c:c + 1],
                                                          bv_[0][:, :], ALU.mult, ALU.add)
                link(last)
                split(w_qv[:, :, :], w_qv_hi, w_qv_lo)

            def weights_o():
                dve.wait_ge(wo_in, 16)
                link(nc.vector.tensor_scalar(w_o, w_o, 0.5, None, ALU.mult))
                split(w_o, w_o_hi, w_o_lo)

            def modulation():
                dve.wait_ge(emb_out, 2 * C)
                link(nc.vector.tensor_scalar(emb[:, 0:C, :], emb[:, 0:C, :], 1.0, None, ALU.add))
                for c in range(C):
                    nc.vector.tensor_scalar(mod_scale[:, c, :], emb[:, c, :], ln2w[:, c:c + 1], None,
                                            ALU.mult)
                    nc.vector.scalar_tensor_tensor(mod_shift[:, c, :], emb[:, c, :], ln2b[:, c:c + 1],
                                                   emb[:, C + c, :], ALU.mult, ALU.add).then_inc(mod_ready, 1)

            def weights_k_o():
                weights_k()
                weights_o()

            def q_tiles(i, par, tiles):
                q = [b[:, 0:D].rearrange("p (h d) -> p h d", d=DH) for b in bqv]
                for t in tiles:
                    wait(dve, v_d, 4 * i + t + 1)
                    wait(dve, qsub_d, 4 * i + t - 3)
                    nc.vector.tensor_reduce(out=qmax[:, t, :], in_=q[t], axis=AX.X, op=ALU.max).then_inc(qmax_d, 1)
                for t in tiles:
                    if t == 0:
                        wait(dve, eqt_d, 2 * i - 2)
                    wait(dve, qmax_d, 4 * i + t + 1)
                    nc.vector.tensor_tensor(q_s[:, par, t, :].rearrange("p (h d) -> p h d", d=DH), q[t],
                                            qmax[:, t, :].unsqueeze(2).broadcast_to([P, HEADS, DH]),
                                            ALU.subtract).then_inc(qsub_d, 1)

            def z_scaled(g):
                for c in range(C):
                    wait(dve, yt_d, 2 * g + c + 1)
                    wait(dve, h_d, 2 * g)
                    nc.vector.tensor_tensor(
                        z_s[:, c, :].rearrange("p (b s) -> p b s", s=SEQ),
                        be[c][:, :].rearrange("p (b s) -> p b s", s=SEQ),
                        mod_scale[:, c, span(g, GB)].unsqueeze(2).broadcast_to([P, GB, SEQ]),
                        ALU.mult).then_inc(zs_d, 1)
                    if isinstance(g, int) and last_step(g + 2):
                        wait(dve, zs_d, 2 * g + c + 1)
                        shift(nc.vector, g, c).then_inc(z_d, 1)

            def body(i, par, N, F, B, O):
                if F:
                    for c in range(C):
                        wait(dve, hi_d, 2 * i + c + 1)
                        nc.vector.tensor_tensor(xt_lo[:, c, :], bt[c][:, :], xt_hi[:, c, :].bitcast(fp32),
                                                ALU.subtract).then_inc(lo_d, 1)
                    if isinstance(i, int) and i == 0:
                        weights_qv()
                for c in range(C):
                    if F:
                        wait(dve, k_d, 2 * i + c + 1)
                        wait(dve, ksub_d, 2 * i + c - 1)
                        kk = bk_[c][:, :].rearrange("p (b s) -> p b s", s=SEQ)
                        nc.vector.tensor_reduce(out=kmax[:, c, :], in_=kk, axis=AX.X, op=ALU.max).then_inc(kmax_d, 1)
                        wait(dve, kmax_d, 2 * i + c + 1)
                        if c == 0:
                            wait(dve, ekt_d, 2 * i - 2)
                        nc.vector.tensor_tensor(k_t[:, par, c, :].rearrange("p (b s) -> p b s", s=SEQ), kk,
                                                kmax[:, c, :].unsqueeze(2).broadcast_to([P, GB, SEQ]),
                                                ALU.subtract).then_inc(ksub_d, 1)
                    if O and c == 0:
                        z_scaled(i - 2)
                if N:
                    x_stats(i + 1, 1 - par)
                if B:
                    g = i - 1
                    wait(dve, att_d, g + 1)
                    wait(dve, qt_d, 2 * g)
                    for e in range(2):
                        sums = be[e][:, 0:GB // 2 * C * AW].rearrange("p (b c n) -> p b c n", c=C, n=AW)
                        nc.vector.reciprocal(rk[:, e, :, :], sums[:, :, :, DH]).then_inc(rk_d, 1)
                    wait(dve, y_d, 4 * g)
                    rows = slice((HC - 1) * DH, P)
                    nc.vector.tensor_copy(kv[rows, 1:GB:2, :, (HC - 1) * AW:HC * AW],
                                          be[1][rows, 0:GB // 2 * C * AW].rearrange(
                                              "p (b c n) -> p b c n", c=C, n=AW)).then_inc(kv_v_d, 1)
                    wait(dve, rk_d, 2 * g + 2)
                    for c in range(C):
                        wait(dve, eqt_d, 2 * g + c + 1)
                        nc.vector.tensor_tensor(
                            q_t[:, c, :].rearrange("p (b e s) -> p b e s", e=2, s=SEQ),
                            bt[c][:, :].rearrange("p (b e s) -> p b e s", e=2, s=SEQ),
                            rk[:, :, :, c].rearrange("p e b -> p b e").unsqueeze(3)
                            .broadcast_to([P, GB // 2, 2, SEQ]), ALU.mult).then_inc(qt_d, 1)
                if O:
                    g = i - 2
                    for c in range(C):
                        wait(dve, th_d, 2 * g + c + 1)
                        wait(dve, hlo_d, 2 * g)
                        nc.vector.scalar_tensor_tensor(h_s[:, c, :], th[:, c, :], 1.0, z_s[:, c, :],
                                                       ALU.add, ALU.mult).then_inc(h_d, 1)
                    if last_step(i):
                        for c in range(C):
                            wait(dve, hhi_d, 2 * g + c + 1)
                            wait(dve, o_d, 2 * g)
                            h_low(nc.vector, c).then_inc(hlo_d, 1)
                if F:
                    q_tiles(i, par, (0, 1))
                if B:
                    g = i - 1
                    y_of = [b[:, 0:C * HC * AW].rearrange("p (h n) -> p h n", n=AW) for b in be + bt]

                    def y_norm(t):
                        wait(dve, rq_d, 4 * g + t + 1)
                        nc.vector.tensor_tensor(y_s[:, t, :].rearrange("p (h d) -> p h d", d=DH),
                                                y_of[t][:, :, 0:DH],
                                                rq[:, t, :].unsqueeze(2).broadcast_to([P, HEADS, DH]),
                                                ALU.mult).then_inc(ys_d, 1)

                    def y_stat(t):
                        wait(dve, ys_d, 4 * g + t + 1)
                        nc.vector.bn_stats(ystat[:, t, :], y_s[:, t, :]).then_inc(ystat_d, 1)

                    wait(dve, yt_d, 2 * g)
                    wait(dve, ys_d, 4 * g)
                    wait(dve, yr_d, 2 * g)
                    for t in range(T):
                        wait(dve, y_d, 4 * g + t + 1)
                        nc.vector.reciprocal(rq[:, t, :], y_of[t][:, :, DH]).then_inc(rq_d, 1)
                        if t > 1:
                            y_stat(t - 2)
                        if t > 0:
                            y_norm(t - 1)
                    y_stat(T - 2)
                    y_norm(T - 1)
                    y_stat(T - 1)
                    for t in range(T):
                        wait_apart(dve, ystat_d, 4 * g + t + 1)
                        nc.vector.bn_aggr(ymv[:, t, :], ystat[:, t, :]).then_inc(ymv_d, 1)
                    wait(dve, yhat_d, 4 * g)
                    wait_apart(dve, ymv_d, 4 * g + 4)
                    nc.vector.tensor_scalar(yr[:, 0, :], ymv[:, :, 1], 1.0, EPS, ALU.mult, ALU.add).then_inc(yve_d, 1)
                    nc.vector.tensor_scalar(yr[:, 2, :], ymv[:, :, 0], -1.0, None, ALU.mult).then_inc(yve_d, 1)
                if isinstance(i, int) and i == 0:
                    modulation()
                if F:
                    q_tiles(i, par, (2, 3))
                if O:
                    g = i - 2
                    wait(dve, xb_d, g + 1)
                    for e in range(2):
                        wait(dve, o_d, 2 * g + e + 1)
                        xg = group_of(x_all, g)[:, :, 2 * e * D:2 * e * D + 2 * D].rearrange("p g n -> p (g n)")
                        nc.vector.tensor_tensor(xg, bv_[e][:, :], xg, ALU.add).then_inc(res_d, 1)

            fold_and_mask()
            steps(dve, body, weights_k_o)

        @block.tensor
        def _(pe):
            def mm(dst, lhsT, rhs, start, stop):
                return nc.tensor.matmul(dst, lhsT, rhs, start=start, stop=stop)

            def beta(dst, w, b0, n):
                for c in range(C):
                    mm(dst[:, 0:n], fold[:, c, :], w[:, c, :], c == 0, False)
                mm(dst[:, 0:n], inv_row[:, :], brow[:, b0:b0 + n], False, True).then_inc(beta_done, 1)

            pe.wait_ge(pool_init, 4)
            pe.wait_ge(fold_ready, C)
            pe.wait_ge(brow_in, 16)
            pe.wait_ge(wk_in, 16)
            beta(bk_[0], w_k, 2 * D, D)
            pe.wait_ge(wqv_in, 32)
            beta(bv_[0], w_qv, 0, 2 * D)

            def emb_products():
                pe.wait_ge(silu_c_ready, 1)
                pe.wait_ge(we_in, 32)
                for j in range(2 * C):
                    for c in range(EC):
                        last = mm(be[1][:, j * BATCH:(j + 1) * BATCH], w_e[c // 2][:, c % 2, j * P:(j + 1) * P],
                                  tanh_c[:, c, :], c == 0, c == EC - 1)
                last.then_inc(emb_done, 1)

            def qv_tile(i, t):
                if t < 2:
                    wait(pe, qsub_d, 4 * i + t - 3)
                    wait(pe, res_d, 2 * (i - 3) + t + 1)
                else:
                    wait(pe, ksub_d, 2 * i + t - 1)
                tok = slice(t * P, t * P + P)
                parts = [(xt_hi, w_qv_hi), (xt_hi, w_qv_lo), (xt_lo, w_qv_hi)]
                for n, (a, w) in enumerate(parts):
                    for c in range(C):
                        last = mm(bqv[t][:, :], a[:, c, tok], w[:, c, :], n + c == 0,
                                  n == len(parts) - 1 and c == C - 1)
                last.then_inc(qv_d, 1)

            def exp_k_transposed(g, par):
                if isinstance(g, int) and g == 0:
                    pe.wait_ge(emb_out, 2 * C)
                    pe.wait_ge(pool_init, 6)
                wait(pe, kexp_d, 2 * g + 2)
                for e in range(2):
                    wait(pe, ys_d, 4 * (g - 1) + e + 1)
                    for t in (2 * e, 2 * e + 1):
                        for c in range(C):
                            last = nc.tensor.transpose(be[e][:, (t % 2) * D + c * P:(t % 2) * D + c * P + P],
                                                       k_t[:, 1 - par, c, t * P:t * P + P], ident[:, :])
                    last.then_inc(ekt_d, 1)

            def y_transposed(g, B):
                wait(pe, yhat_d, 4 * g + 4)
                for c in range(C):
                    if B:
                        wait(pe, ek_d, 2 * g + c + 3)
                    for t in range(T):
                        last = nc.tensor.transpose(be[c][:, t * P:t * P + P], y_s[:, t, c * P:c * P + P],
                                                   ident[:, :])
                    last.then_inc(yt_d, 1)

            def body(i, par, N, F, B, O):
                if F:
                    for c in range(C):
                        if c == 0:
                            wait(pe, xhat_d, 4 * i + 4)
                        wait(pe, ys_d, 4 * (i - 2) + c + 3)
                        for t in range(T):
                            last = nc.tensor.transpose(bt[c][:, t * P:t * P + P], xhat[:, par, t, c * P:c * P + P],
                                                       ident[:, :])
                        last.then_inc(xt_d, 1)
                if B:
                    exp_k_transposed(i - 1, par)
                for c in range(C):
                    if F:
                        out_c = slice(c * P, c * P + P)
                        wait_apart(pe, qsub_d, 4 * i + c - 1)
                        if isinstance(i, int) and i == 0 and c == 0:
                            pe.wait_ge(n_rows_in, 32)
                            pe.wait_ge(weights_ready, 1)
                        mm(bk_[c][:, :], ones2[:, :], n_row[:, span(i, GT)], True, False)
                        wait(pe, hi_d, 2 * i + 2)
                        for j in range(C):
                            mm(bk_[c][:, :], w_k_hi[:, j, out_c], xt_hi[:, j, :], False, False)
                            mm(bk_[c][:, :], w_k_lo[:, j, out_c], xt_hi[:, j, :], False, False)
                        wait(pe, lo_d, 2 * i + 2)
                        for j in range(C):
                            last = mm(bk_[c][:, :], w_k_hi[:, j, out_c], xt_lo[:, j, :], False, j == C - 1)
                        last.then_inc(k_d, 1)
                    if O and c == 0:
                        y_transposed(i - 2, B)
                if B:
                    g = i - 1
                    wait(pe, qexp_d, 2 * g + 2)
                    for c in range(C):
                        wait(pe, lo_d, 2 * (g + 1) + c + 1 if F else 2 * G)
                        for t in range(T):
                            last = nc.tensor.transpose(bt[c][:, t * P:t * P + P], q_s[:, 1 - par, t, c * P:c * P + P],
                                                       ident[:, :])
                        last.then_inc(eqt_d, 1)
                if B:
                    g = i - 1
                    wait(pe, ek_d, 2 * g + 2)
                    wait(pe, zs_d, 2 * g)
                    wait_apart(pe, v_d, 4 * g + 4)
                    for b in range(GB):
                        t, e = b // 2, b % 2
                        rows = slice(e * SEQ, e * SEQ + SEQ)
                        for c in range(C):
                            col = (t * C + c) * AW
                            for h in range(HC):
                                ch = c * P + h * DH
                                last = mm(be[e][h * DH:h * DH + DH, col:col + AW], e_k[rows, t, ch:ch + DH],
                                          v_s[rows, 1 - par, t, c * HC + h, :], True, True)
                    last.then_inc(att_d, 1)
                if F:
                    if isinstance(i, int) and i == 0:
                        emb_products()
                        pe.wait_ge(weights_ready, 3)
                    qv_tile(i, 0)
                    qv_tile(i, 1)
                if B:
                    g = i - 1
                    wait(pe, kv_d, 7 * g + 7)
                    wait(pe, kv_v_d, g + 1)
                    wait(pe, qt_d, 2 * g + 2)
                    for t in range(T):
                        yb = be[t] if t < 2 else bt[t - 2]
                        for c in range(C):
                            for e in range(2):
                                last = mm(yb[e * SEQ:e * SEQ + SEQ, c * HC * AW:(c + 1) * HC * AW],
                                          q_t[:, c, t * P + e * SEQ:t * P + e * SEQ + SEQ], kv[:, 2 * t + e, c, :],
                                          True, True)
                        last.then_inc(y_d, 1)
                if F:
                    qv_tile(i, 2)
                    qv_tile(i, 3)
                if O:
                    g = i - 2
                    wait(pe, hhi_d, 2 * g + 2)
                    for e in range(2):
                        wait(pe, qsub_d, 4 * i + e + 1 if F else 4 * G)
                        if not F:
                            wait(pe, res_d, 2 * g + e - 1)
                        for t in (2 * e, 2 * e + 1):
                            tok = slice(t * P, t * P + P)
                            dst = bv_[e][:, (t % 2) * D:(t % 2) * D + D]
                            for c in range(C):
                                mm(dst, h_hi[:, c, tok], w_o_hi[:, c, :], c == 0, False)
                                mm(dst, h_hi[:, c, tok], w_o_lo[:, c, :], False, False)
                            if t == 0:
                                wait(pe, hlo_d, 2 * g + 2)
                            for c in range(C):
                                last = mm(dst, h_lo[:, c, tok], w_o_hi[:, c, :], False, c == C - 1)
                        last.then_inc(o_d, 1)

            steps(pe, body)


_ARGS = ["x", "cond_t", "columns_in", "b_qvk", "mask_rows", "wq", "wk", "wv", "w_emb", "w_out", "b_out"]


def kernel(x, cond_2048, mask_BxSx1_fk1, L0_cond_ln_w, L0_cond_ln_b, L0_cond_Wq, L0_cond_bq, L0_cond_Wk, L0_cond_bk,
           L0_cond_Wv, L0_cond_bv, L0_cond_W_emb, L0_cond_b_emb, L0_cond_ln2_w, L0_cond_ln2_b, L0_cond_W_out,
           L0_cond_b_out):
    import concourse.bacc as _bacc
    from concourse.bass_utils import run_bass_kernel_spmd as _run

    b, s, d = x.shape
    P = 128

    def columns(v):
        return np.ascontiguousarray(np.asarray(v).reshape(-1, P).T)

    mask = np.asarray(mask_BxSx1_fk1)
    vectors = [L0_cond_ln_w, L0_cond_ln_b, L0_cond_ln2_w, L0_cond_ln2_b, L0_cond_b_emb, mask.reshape(-1)]
    arrays = [np.asarray(x).reshape(b * s, d), np.ascontiguousarray(np.asarray(cond_2048).T),
              np.concatenate([columns(v) for v in vectors], axis=1),
              np.concatenate([np.asarray(v) for v in (L0_cond_bq, L0_cond_bv, L0_cond_bk)]), mask.reshape(b, s),
              L0_cond_Wq, L0_cond_Wk, L0_cond_Wv, L0_cond_W_emb, L0_cond_W_out, L0_cond_b_out]
    nc = _bacc.Bacc("TRN2", target_bir_lowering=False, num_devices=1)
    feed, args = {}, []
    for name, a in zip(_ARGS, arrays):
        a = np.ascontiguousarray(a)
        feed[f"in_{name}"] = a
        args.append(nc.dram_tensor(f"in_{name}", a.shape, mybir.dt.from_np(a.dtype), kind="ExternalInput").ap())
    out = nc.dram_tensor("out_0", (b * s, d), mybir.dt.float32, kind="ExternalOutput").ap()
    build_layer(nc, *args, out)
    r = _run(nc, [feed], core_ids=[0])
    return r.results[0]["out_0"].reshape(b, s, d)
```
